# Optimizing a Trainium2 kernel written in Bass

```python
import numpy as np
import jax
import jax.numpy as jnp

def _softmax(x, axis=-1):
    return jax.nn.softmax(x, axis=axis)

def _gelu(x):
    return jax.nn.gelu(x, approximate=True)

def _silu(x):
    return jax.nn.silu(x)

def _sigmoid(x):
    return jax.nn.sigmoid(x)

def _layernorm(x, axis=-1, eps=1e-05):
    m = jnp.mean(x, axis=axis, keepdims=True)
    v = jnp.var(x, axis=axis, keepdims=True)
    return (x - m) / jnp.sqrt(v + eps)

def _scatter_add(tgt, idx, src, axis=0):
    return tgt.at[idx].add(src)

def _segment_sum(src, seg, n):
    return jax.ops.segment_sum(src, seg, n)
kernel_name = 'mk_adj_resnorm_d1_adj_r2_d002f5'

def setup_inputs(seed: int=0):
    np.random.seed(seed)
    _w = jnp.asarray

    def _rec_inputs():
        import jax
        import jax.numpy as jnp
        _gk = jax.random.key(seed)
        x = -0.001003 + 1 * jax.random.normal(jax.random.fold_in(_gk, 1), (8192, 128), jnp.float32)
        _a = jax.random.bernoulli(jax.random.fold_in(_gk, 2), 0.00195312, (8192, 8192))
        _a = jnp.logical_or(_a, jnp.swapaxes(_a, -1, -2))
        _a = jnp.logical_or(_a, jnp.eye(8192, dtype=bool))
        _af = _a.astype(jnp.float32)
        _af = _af * jax.random.uniform(jax.random.fold_in(_gk, 3), (8192, 8192), jnp.float32, 0.05, 0.999999)
        adj = _af
        return (x, adj)
    x, adj = _rec_inputs()

    def _L0_gnn_setup():
        import jax, jax.numpy as jnp
        import numpy as np
        N = 3072
        HID = 128
        T = 350
        DENSITY = 0.05
        key = jax.random.key(seed)
        k1, k2, k3, k4, k5, k6 = jax.random.split(key, 6)
        h = jax.random.normal(k1, (N, HID), dtype=jnp.float32)
        a = jax.random.uniform(k2, (N, N), dtype=jnp.float32)
        mask = jax.random.uniform(k3, (N, N)) < DENSITY
        adj = jnp.where(mask, a, 0.0)
        simlar = jax.random.normal(k4, (N, N), dtype=jnp.float32)
        s = 1.0 / np.sqrt(HID)
        W_proj = jax.random.uniform(k5, (HID, HID), minval=-s, maxval=s, dtype=jnp.float32)
        b_proj = jnp.zeros((HID,), dtype=jnp.float32)
        W_gcn = jax.random.uniform(k6, (HID, HID), minval=-s, maxval=s, dtype=jnp.float32)
        b_gcn = jnp.zeros((HID,), dtype=jnp.float32)
        return {'h': h, 'adj': adj, 'simlar': simlar, 'W_proj': W_proj, 'b_proj': b_proj, 'W_gcn': W_gcn, 'b_gcn': b_gcn}
    _L0_gnn_all = _L0_gnn_setup()
    _L0_gnn_in = {k: v for k, v in _L0_gnn_all.items() if k in ('W_proj', 'b_proj', 'W_gcn', 'b_gcn')}
    del _L0_gnn_all
    return {'x': x, 'adj': adj, 'L0_gnn_W_proj': _L0_gnn_in['W_proj'], 'L0_gnn_b_proj': _L0_gnn_in['b_proj'], 'L0_gnn_W_gcn': _L0_gnn_in['W_gcn'], 'L0_gnn_b_gcn': _L0_gnn_in['b_gcn']}

def reference(x, adj, L0_gnn_W_proj, L0_gnn_b_proj, L0_gnn_W_gcn, L0_gnn_b_gcn):
    import jax
    import jax.numpy as jnp

    def _L0_gnn_ref(h, adj, simlar, W_proj, b_proj, W_gcn, b_gcn):
        import jax, jax.numpy as jnp
        import numpy as np
        N = 3072
        HID = 128
        T = 350
        DENSITY = 0.05
        sim = jnp.tanh(adj * simlar)
        filt = sim * (adj > 0).astype(sim.dtype)
        vals, idx = jax.lax.top_k(filt, T)
        nnz = jnp.sum(filt != 0, axis=1)
        keep = jnp.arange(T)[None, :] < nnz[:, None]
        rows = jnp.arange(filt.shape[0])[:, None]
        new_adj = jnp.zeros_like(filt).at[rows, idx].set(jnp.where(keep, vals, 0.0))
        h2 = jnp.tanh(h @ W_proj + b_proj)
        feat = jax.nn.relu(new_adj @ (h2 @ W_gcn) + b_gcn)
        return feat
    x = _layernorm(x + _L0_gnn_ref(x, adj, adj, L0_gnn_W_proj, L0_gnn_b_proj, L0_gnn_W_gcn, L0_gnn_b_gcn), axis=-1)
    return x

_drawn_inputs = setup_inputs


def setup_inputs(seed=0):
    import zlib

    import numpy as np

    out = dict(_drawn_inputs(seed))
    spreads = {'L0_gnn_b_proj': (0.0, 0.1), 'L0_gnn_b_gcn': (0.0, 0.1)}
    factors = {}
    for name, (base, spread) in spreads.items():
        noise = np.random.default_rng([zlib.crc32(name.encode()), seed]).standard_normal(out[name].shape)
        drawn = base * np.exp(spread * noise) if base else spread * noise
        out[name] = jnp.asarray(drawn.astype(out[name].dtype))
    for name, factor in factors.items():
        out[name] = (out[name] * factor).astype(out[name].dtype)
    return out
```

```python
from contextlib import ExitStack

import concourse.bass as bass
from concourse import mybir

P = 128
D = 128
TOPK = 350
EPS = 1e-5
IB = 1024
TC = 4
BANK = 512
BANKS = IB // BANK
GROUPS = IB // P
SLOTS = 8
SQUARE_EVERY = 4
FOLD_LAG = 2
MARK_LAG = 3
COUNT_LAG = 3
MARKS = 4
EARLY = 2

ALU = mybir.AluOpType
ACT = mybir.ActivationFunctionType
F32 = mybir.dt.float32
BF16 = mybir.dt.bfloat16
I32 = mybir.dt.int32
AX_X = mybir.AxisListType.X


def top_k_graph_layer(
    nc: bass.Bass,
    adj_tiles: bass.AP,
    x: bass.AP,
    xT: bass.AP,
    w_proj: bass.AP,
    b_proj: bass.AP,
    w_gcn: bass.AP,
    b_gcn: bass.AP,
    identity: bass.AP,
    out: bass.AP,
):
    N = x.shape[0]
    NIB = N // IB
    NT = N // (TC * P)
    R = min(SLOTS, NT)
    NTILES = NIB * NT
    assert N % IB == 0 and NT % R == 0 and x.shape[1] == D == P and BANK == TC * P
    ROWT = N // P

    x_rows = x.rearrange("(b k p) d -> b p k d", k=GROUPS, p=P)
    out_rows = out.rearrange("(b k p) d -> b p k d", k=GROUPS, p=P)
    adj_cols = adj_tiles.rearrange("b t p c i -> b p t c i")

    with ExitStack() as ctx:
        def sb(name, shape, dt):
            return ctx.enter_context(nc.sbuf_tensor(name, shape, dt))

        def psum(name, shape, dt):
            return ctx.enter_context(nc.psum_tensor(name, shape, dt))

        def sem(name):
            return ctx.enter_context(nc.semaphore(name))

        ring = sb("ring", [P, R, TC, IB], F32)
        v_sb = sb("v_sb", [P, NT, TC * D], F32)
        pair_sum = sb("pair_sum", [P, 2, IB], BF16)
        four_sum = sb("four_sum", [P, 2, IB], BF16)
        mark = sb("mark", [P, MARKS, IB], BF16)
        ones = sb("ones", [P, P], BF16)
        ident = sb("ident", [P, P], F32)
        wp_sb = sb("wp_sb", [P, D], F32)
        wg_sb = sb("wg_sb", [P, D], F32)
        bias = sb("bias", [P, 2], F32)
        featT = sb("featT", [P, IB], F32)
        x_sb = sb("x_sb", [P, GROUPS, D], F32)
        y_sb = sb("y_sb", [P, GROUPS, D], F32)
        norm_sb = sb("norm_sb", [P, GROUPS, D], F32)
        row_sum = sb("row_sum", [P, GROUPS], F32)
        neg_mean = sb("neg_mean", [P, GROUPS], F32)
        sq_sum = sb("sq_sum", [P, GROUPS], F32)
        var = sb("var", [P, 2, GROUPS], F32)
        rstd0 = sb("rstd0", [P, GROUPS], F32)
        newton = sb("newton", [P, 4, GROUPS], F32)
        rstd = sb("rstd", [P, GROUPS], F32)
        shift = sb("shift", [P, GROUPS], F32)
        pool_const = sb("pool_const", [P, 5, GROUPS], F32)
        bound = sb("bound", [P, 1], F32)
        above = sb("above", [P, 1], BF16)
        select_flag = sb("select_flag", [P, 1], I32)
        tau = sb("tau", [P, 1], I32)
        candidate = sb("candidate", [P, 1], I32)
        keep_bit = sb("keep_bit", [P, 1], I32)
        bit = sb("bit", [P, 2], F32)
        bit_int = sb("bit_int", [P, 1], I32)
        n_at_least = sb("n_at_least", [P, 1], F32)
        n_above = sb("n_above", [P, 1], F32)
        room = sb("room", [P, 1], F32)

        accT = psum("accT", [P, BANKS, BANK], F32)
        counts = psum("counts", [P, BANK], F32)
        turned = psum("turned", [P, 2, BANK], F32)
        v_ps = psum("v_ps", [P, 2, BANK], F32)

        half = NT * TC * P
        flat = ring[:, :, :, :].rearrange("p s c i -> p (s c i)")
        cols = flat[:, 0:half]
        rows = flat[:, half:2 * half]
        prefix = flat[:, 2 * half:3 * half]
        equal = flat[:, 3 * half:3 * half + half // 2].bitcast(BF16)
        passed = flat[:, 3 * half + half // 2:4 * half].bitcast(BF16)

        weights_loaded = sem("weights_loaded")
        xT_loaded = [sem(f"xT_loaded{q}") for q in range(NT)]
        tile_loaded = [sem(f"tile_loaded{s}") for s in range(R)]
        constants_set = sem("constants_set")
        hidden_product = sem("hidden_product")
        hidden_ready = sem("hidden_ready")
        v_product = sem("v_product")
        v_ready = sem("v_ready")
        squared = sem("squared")
        act_squared = sem("act_squared")
        filtered = sem("filtered")
        paired = sem("paired")
        folded = sem("folded")
        marked = sem("marked")
        counted = sem("counted")
        bank_product = sem("bank_product")
        feat_ready = sem("feat_ready")
        feat_turned = sem("feat_turned")
        x_loaded = sem("x_loaded")
        added = sem("added")
        summed = sem("summed")
        mean_ready = sem("mean_ready")
        sq_summed = sem("sq_summed")
        pool_step = sem("pool_step")
        rstd_ready = sem("rstd_ready")
        normed = sem("normed")
        stored = sem("stored")
        flag_step = sem("flag_step")
        rows_above = sem("rows_above")
        flag_ready = sem("flag_ready")
        cols_loaded = sem("cols_loaded")
        cols_squared = sem("cols_squared")
        cols_filtered = sem("cols_filtered")
        group_turned = sem("group_turned")
        group_copied = sem("group_copied")
        search_step = sem("search_step")
        rows_kept = sem("rows_kept")
        group_returned = sem("group_returned")
        group_restored = sem("group_restored")
        select_done = sem("select_done")

        ACT_SQUARES = NT // SQUARE_EVERY

        def act_squares(t):
            return t % SQUARE_EVERY == SQUARE_EVERY - 1

        POOL_STEPS = 8
        POOL_CONSTS = (-1.0 / D, 1.0 / D, EPS, -0.5, 1.5)

        AT_EVACUATE, AT_TURN, AT_ADD, AT_SUM, AT_SQUARE, AT_NORM = (
            (1, 2, 6, 7, 9, 11) if NT >= 16 else (1, 2, 2, 3, 3, 3))

        def load_x(sp, e, source, groups):
            sp.dma_start(x_sb[:, 0:groups, :], source).then_inc(x_loaded, 16)

        def add_x(dve, e, groups):
            dve.wait_ge(feat_turned, e + 1)
            dve.wait_ge(x_loaded, 16 * (e + 1))
            nc.vector.tensor_tensor(
                y_sb[:, 0:groups, :], turned[:, :, :].rearrange("p a (k d) -> p (a k) d", d=D)[:, 0:groups, :],
                x_sb[:, 0:groups, :], ALU.add).then_inc(added, 1)

        def sum_rows(act, e, groups):
            act.wait_ge(added, e + 1)
            for k in range(groups):
                last = nc.scalar.activation(norm_sb[:, k, :], y_sb[:, k, :], ACT.Identity,
                                            accum_out=row_sum[:, k:k + 1])
            last.then_inc(summed, 1)

        def sum_squares(act, e, groups):
            act.wait_ge(mean_ready, e + 1)
            for k in range(groups):
                last = nc.scalar.activation(norm_sb[:, k, :], y_sb[:, k, :], ACT.Square,
                                            bias=neg_mean[:, k:k + 1], accum_out=sq_sum[:, k:k + 1])
            last.then_inc(sq_summed, 1)

        def normalise(act, e, target, groups):
            act.wait_ge(rstd_ready, e + 1)
            for k in range(groups):
                last = nc.scalar.activation(norm_sb[:, k, :], y_sb[:, k, :], ACT.Identity,
                                            bias=shift[:, k:k + 1], scale=rstd[:, k:k + 1])
            last.then_inc(normed, 1)
            act.wait_ge(normed, e + 1)
            act.dma_start(target, norm_sb[:, 0:groups, :]).then_inc(stored, 16)

        def statistics(pool, e, groups):
            g = slice(0, groups)
            minus_1_d, one_d, eps, minus_half, three_halves = (pool_const[:, n, g] for n in range(len(POOL_CONSTS)))
            pool.wait_ge(summed, e + 1)
            nc.gpsimd.tensor_tensor(neg_mean[:, g], row_sum[:, g], minus_1_d, ALU.mult).then_inc(mean_ready, 1)
            pool.wait_ge(sq_summed, e + 1)
            nc.gpsimd.tensor_tensor(var[:, 0, g], sq_sum[:, g], one_d, ALU.mult).then_inc(pool_step, 1)
            pool.wait_ge(pool_step, POOL_STEPS * e + 1)
            nc.gpsimd.tensor_tensor(var[:, 1, g], var[:, 0, g], eps, ALU.add).then_inc(pool_step, 1)
            pool.wait_ge(pool_step, POOL_STEPS * e + 2)
            nc.gpsimd.tensor_tensor(rstd0[:, g], var[:, 1, g], minus_half, ALU.pow).then_inc(pool_step, 1)
            nc.gpsimd.tensor_tensor(newton[:, 0, g], var[:, 1, g], minus_half, ALU.mult).then_inc(pool_step, 1)
            pool.wait_ge(pool_step, POOL_STEPS * e + 4)
            nc.gpsimd.tensor_tensor(newton[:, 1, g], newton[:, 0, g], rstd0[:, g], ALU.mult).then_inc(pool_step, 1)
            pool.wait_ge(pool_step, POOL_STEPS * e + 5)
            nc.gpsimd.tensor_tensor(newton[:, 2, g], newton[:, 1, g], rstd0[:, g], ALU.mult).then_inc(pool_step, 1)
            pool.wait_ge(pool_step, POOL_STEPS * e + 6)
            nc.gpsimd.tensor_tensor(newton[:, 3, g], newton[:, 2, g], three_halves, ALU.add).then_inc(pool_step, 1)
            pool.wait_ge(pool_step, POOL_STEPS * e + 7)
            nc.gpsimd.tensor_tensor(rstd[:, g], newton[:, 3, g], rstd0[:, g], ALU.mult).then_inc(pool_step, 1)
            pool.wait_ge(pool_step, POOL_STEPS * e + 8)
            nc.gpsimd.tensor_tensor(shift[:, g], neg_mean[:, g], rstd[:, g], ALU.mult).then_inc(rstd_ready, 1)

        block = ctx.enter_context(nc.Block())

        @block.sync
        def _(sp):
            def load_tile(b, t, freed):
                s = t % R
                T = b * NT + t
                if freed:
                    sp.wait_ge(bank_product, BANKS * (T - R + 1))
                    sp.wait_ge(paired, T - R + 1)
                sp.dma_start(ring[:, s, :, :], adj_tiles[b, t]).then_inc(tile_loaded[s], 16)

            for dst, src in ((wp_sb[:, :], w_proj), (wg_sb[:, :], w_gcn), (bias[:, 0:1], b_proj),
                             (bias[:, 1:2], b_gcn), (ident[:, :], identity)):
                sp.dma_start(dst, src).then_inc(weights_loaded, 16)
            for q in range(NT):
                sp.dma_start(v_sb[:, q, :], xT[:, q * TC * P:(q + 1) * TC * P]).then_inc(xT_loaded[q], 16)
            for t in range(NT):
                load_tile(0, t, t >= R)
            with sp.Fori(1, NIB) as b:
                load_x(sp, b - 1, x_rows[b - 1], GROUPS)
                for t in range(NT):
                    if t == NT - 1:
                        sp.wait_ge(added, b)
                    load_tile(b, t, True)
            load_x(sp, NIB - 1, x_rows[NIB - 1], GROUPS)

            sp.wait_ge(flag_ready, 1)
            with sp.If(sp.value_load(select_flag[0:1, 0:1], min_val=0, max_val=1) > 0):
                with sp.Fori(0, NIB) as b:
                    with sp.Fori(0, GROUPS) as k:
                        r = b * GROUPS + k
                        sp.wait_ge(added, NIB + r)
                        for t in range(NT):
                            sp.dma_start(cols.rearrange("p (t c i) -> p t c i", t=NT, c=TC)[:, t],
                                         adj_tiles[b, t, :, :, bass.ds(k * P, P)]).then_inc(cols_loaded, 16)
                        load_x(sp, NIB + r, x_rows[b, :, bass.ds(k, 1), :], 1)

        @block.gpsimd
        def _(pool):
            nc.gpsimd.memset(ones[:, :], 1.0).then_inc(constants_set, 1)
            for n, value in enumerate(POOL_CONSTS):
                nc.gpsimd.memset(pool_const[:, n, :], value).then_inc(constants_set, 1)
            pool.wait_ge(constants_set, 1 + len(POOL_CONSTS))
            with pool.Fori(0, NIB) as b:
                statistics(pool, b, GROUPS)

            pool.wait_ge(flag_ready, 1)
            with pool.If(pool.value_load(select_flag[0:1, 0:1], min_val=0, max_val=1) > 0):
                with pool.Fori(0, ROWT) as r:
                    statistics(pool, NIB + r, 1)

        @block.scalar
        def _(act):
            def hidden(q):
                act.wait_ge(hidden_product, q + 1)
                nc.scalar.activation(v_sb[:, q, :], turned[:, q % 2, :], ACT.Tanh,
                                     bias=bias[:, 0:1]).then_inc(hidden_ready, 1)

            def tanh_tile(b, t):
                act.wait_ge(squared, b * NT + t + 1)
                if act_squares(t):
                    nc.scalar.activation(ring[:, t % R, :, :], ring[:, t % R, :, :],
                                         ACT.Square).then_inc(act_squared, 1)
                    act.wait_ge(act_squared, ACT_SQUARES * b + t // SQUARE_EVERY + 1)
                nc.scalar.activation(ring[:, t % R, :, :], ring[:, t % R, :, :], ACT.Tanh).then_inc(filtered, 1)

            def copy_v(q):
                act.wait_ge(v_product, q + 1)
                nc.scalar.copy(v_sb[:, q, :], v_ps[:, q % 2, :]).then_inc(v_ready, 1)

            def mark_tile(b, t, reused):
                T = b * NT + t
                act.wait_ge(folded, T + 1)
                if reused:
                    act.wait_ge(counted, T - MARKS + 1)
                nc.scalar.activation(mark[:, t % MARKS, :], four_sum[:, t % 2, :], ACT.Sign).then_inc(marked, 1)

            def evacuate(b):
                for a in range(BANKS):
                    act.wait_ge(bank_product, BANKS * ((b + 1) * NT - 1) + a + 1)
                    nc.scalar.activation(featT[:, a * BANK:(a + 1) * BANK], accT[:, a, :], ACT.Relu,
                                         bias=bias[:, 1:2]).then_inc(feat_ready, 1)

            def block_steps(b, first):
                for t in range(NT):
                    if not first or t >= EARLY:
                        tanh_tile(b, t)
                    if t >= MARK_LAG:
                        mark_tile(b, t - MARK_LAG, not first or t - MARK_LAG >= MARKS)
                    elif not first:
                        mark_tile(b - 1, t - MARK_LAG + NT, True)
                    if not first:
                        if t == AT_EVACUATE:
                            evacuate(b - 1)
                        if t == AT_SUM:
                            sum_rows(act, b - 1, GROUPS)
                        if t == AT_SQUARE:
                            sum_squares(act, b - 1, GROUPS)
                        if t == AT_NORM:
                            normalise(act, b - 1, out_rows[b - 1], GROUPS)
                if not first:
                    act.wait_ge(feat_turned, b)
                    act.wait_ge(stored, 16 * b)

            act.wait_ge(weights_loaded, 16 * 5)
            hidden(0)
            hidden(1)
            for q in range(NT):
                copy_v(q)
                if q + 2 < NT:
                    hidden(q + 2)
                if q >= NT - EARLY:
                    tanh_tile(0, q - (NT - EARLY))
            block_steps(0, True)
            with act.Fori(1, NIB) as b:
                block_steps(b, False)
            last_b = NIB - 1
            for t in range(NT - MARK_LAG, NT):
                mark_tile(last_b, t, True)
            evacuate(last_b)
            sum_rows(act, last_b, GROUPS)
            sum_squares(act, last_b, GROUPS)
            normalise(act, last_b, out_rows[last_b], GROUPS)
            act.wait_ge(stored, 16 * NIB)

            act.wait_ge(flag_ready, 1)
            with act.If(act.value_load(select_flag[0:1, 0:1], min_val=0, max_val=1) > 0):
                with act.Fori(0, NIB) as b:
                    with act.Fori(0, GROUPS) as k:
                        r = b * GROUPS + k
                        e = NIB + r
                        act.wait_ge(cols_squared, r + 1)
                        nc.scalar.activation(cols, cols, ACT.Tanh).then_inc(cols_filtered, 1)
                        act.wait_ge(select_done, r + 1)
                        nc.scalar.activation(featT[:, 0:P], accT[:, 0, 0:P], ACT.Relu,
                                             bias=bias[:, 1:2]).then_inc(feat_ready, 1)
                        sum_rows(act, e, 1)
                        sum_squares(act, e, 1)
                        normalise(act, e, out_rows[b, :, bass.ds(k, 1), :], 1)
                        act.wait_ge(stored, 16 * (e + 1))

        @block.vector
        def _(dve):
            def square_tile(b, t):
                s = t % R
                dve.wait_ge(tile_loaded[s], 16 * (b * (NT // R) + t // R + 1))
                if act_squares(t):
                    nc.vector.tensor_scalar(ring[:, s, :, :], ring[:, s, :, :], 0.0, None, ALU.max).then_inc(squared, 1)
                    return
                nc.vector.scalar_tensor_tensor(out=ring[:, s, :, :], in0=ring[:, s, :, :], scalar=0.0,
                                               in1=ring[:, s, :, :], op0=ALU.max, op1=ALU.mult).then_inc(squared, 1)

            def fold_tile(b, t, before):
                T = b * NT + t
                s = t % R
                dve.wait_ge(filtered, T + 1)
                if before >= 1:
                    dve.wait_ge(folded, T)
                nc.vector.tensor_tensor(pair_sum[:, :, :], ring[:, s, 0:2, :], ring[:, s, 2:4, :],
                                        ALU.add).then_inc(paired, 1)
                dve.wait_ge(paired, T + 1)
                if before >= 2:
                    dve.wait_ge(marked, T - 1)
                nc.vector.tensor_tensor(four_sum[:, t % 2, :], pair_sum[:, 0, :], pair_sum[:, 1, :],
                                        ALU.add).then_inc(folded, 1)

            def block_steps(b, first):
                for t in range(NT):
                    square_tile(b, t)
                    if t >= FOLD_LAG:
                        fold_tile(b, t - FOLD_LAG, min(t - FOLD_LAG, 2) if first else 2)
                    elif not first:
                        fold_tile(b - 1, t - FOLD_LAG + NT, 2)
                    if not first and t == AT_ADD:
                        add_x(dve, b - 1, GROUPS)
                if not first:
                    dve.wait_ge(normed, b)

            block_steps(0, True)
            with dve.Fori(1, NIB) as b:
                block_steps(b, False)
            for t in range(NT - FOLD_LAG, NT):
                fold_tile(NIB - 1, t, 2)
            add_x(dve, NIB - 1, GROUPS)
            dve.wait_ge(counted, NTILES)
            nc.vector.reduce_max(bound[:, 0:1], counts[:, 0:ROWT], AX_X).then_inc(flag_step, 1)
            dve.wait_ge(flag_step, 1)
            nc.vector.tensor_scalar(above[:, :], bound[:, 0:1], TOPK / TC, None, ALU.is_gt).then_inc(flag_step, 1)
            dve.wait_ge(rows_above, 1)
            nc.vector.tensor_scalar(select_flag[:, :], counts[:, ROWT:ROWT + 1], 0.5, None,
                                    ALU.is_gt).then_inc(flag_ready, 1)

            dve.wait_ge(flag_ready, 1)
            with dve.If(dve.value_load(select_flag[0:1, 0:1], min_val=0, max_val=1) > 0):
                BITS = 30
                STEPS = 6 * BITS + 8
                with dve.Fori(0, ROWT) as r:
                    dve.wait_ge(cols_loaded, 16 * NT * (r + 1))
                    nc.vector.scalar_tensor_tensor(out=cols, in0=cols, scalar=0.0, in1=cols, op0=ALU.max,
                                                   op1=ALU.mult).then_inc(cols_squared, 1)
                    for q in range(NT):
                        dve.wait_ge(group_turned, NT * r + q + 1)
                        nc.vector.tensor_copy(rows[:, q * BANK:(q + 1) * BANK], turned[:, q % 2, :]).then_inc(group_copied, 1)
                    nc.vector.memset(tau[:, :], 0).then_inc(search_step, 1)
                    dve.wait_ge(group_copied, NT * (r + 1))
                    nc.vector.memset(bit[:, 0:1], float(2 ** (BITS - 1))).then_inc(search_step, 1)
                    with dve.Fori(0, BITS) as n:
                        s0 = STEPS * r + 6 * n + 2
                        dve.wait_ge(search_step, s0)
                        nc.vector.tensor_copy(bit_int[:, :], bit[:, 0:1]).then_inc(search_step, 1)
                        dve.wait_ge(search_step, s0 + 1)
                        nc.vector.tensor_tensor(candidate[:, :], tau[:, :], bit_int[:, :],
                                                ALU.bitwise_or).then_inc(search_step, 1)
                        dve.wait_ge(search_step, s0 + 2)
                        nc.vector.tensor_scalar(passed, rows, candidate[:, :].bitcast(F32), None, ALU.is_ge, ALU.add,
                                                accum_out=n_at_least[:, :]).then_inc(search_step, 1)
                        dve.wait_ge(search_step, s0 + 3)
                        nc.vector.scalar_tensor_tensor(out=keep_bit[:, :], in0=n_at_least[:, :], scalar=float(TOPK),
                                                       in1=bit[:, 0:1], op0=ALU.is_ge, op1=ALU.mult).then_inc(search_step, 1)
                        dve.wait_ge(search_step, s0 + 4)
                        nc.vector.tensor_tensor(tau[:, :], tau[:, :], keep_bit[:, :], ALU.bitwise_or).then_inc(search_step, 1)
                        nc.vector.tensor_scalar(bit[:, 0:1], bit[:, 0:1], 0.5, None, ALU.mult).then_inc(search_step, 1)
                    s1 = STEPS * r + 6 * BITS + 2
                    tau_f = tau[:, :].bitcast(F32)
                    dve.wait_ge(search_step, s1)
                    nc.vector.tensor_scalar(passed, rows, tau_f, None, ALU.is_gt, ALU.add,
                                            accum_out=n_above[:, :]).then_inc(search_step, 1)
                    nc.vector.tensor_scalar(equal, rows, tau_f, None, ALU.is_equal).then_inc(search_step, 1)
                    dve.wait_ge(search_step, s1 + 2)
                    nc.vector.tensor_scalar(room[:, :], n_above[:, :], -1.0, float(TOPK), ALU.mult,
                                            ALU.add).then_inc(search_step, 1)
                    nc.vector.tensor_tensor_scan(prefix, equal, equal, 0.0, ALU.add, ALU.bypass).then_inc(search_step, 1)
                    dve.wait_ge(search_step, s1 + 4)
                    nc.vector.scalar_tensor_tensor(out=passed, in0=prefix, scalar=room[:, 0:1], in1=equal,
                                                   op0=ALU.is_le, op1=ALU.mult).then_inc(search_step, 1)
                    dve.wait_ge(search_step, s1 + 5)
                    nc.vector.scalar_tensor_tensor(out=prefix, in0=rows, scalar=tau_f, in1=passed,
                                                   op0=ALU.is_gt, op1=ALU.add).then_inc(search_step, 1)
                    dve.wait_ge(search_step, s1 + 6)
                    nc.vector.tensor_tensor(rows, rows, prefix, ALU.mult).then_inc(rows_kept, 1)
                    for q in range(NT):
                        dve.wait_ge(group_returned, NT * r + q + 1)
                        nc.vector.tensor_copy(cols[:, q * BANK:(q + 1) * BANK], turned[:, q % 2, :]).then_inc(group_restored, 1)
                    add_x(dve, NIB + r, 1)
                    dve.wait_ge(normed, NIB + r + 1)

        @block.tensor
        def _(pe):
            def hidden(q):
                pe.wait_ge(xT_loaded[q], 16)
                if q >= 2:
                    pe.wait_ge(hidden_ready, q - 1)
                nc.tensor.matmul(turned[:, q % 2, :], wp_sb[:, :], v_sb[:, q, :], start=True,
                                 stop=True).then_inc(hidden_product, 1)

            def make_v(q):
                pe.wait_ge(hidden_ready, q + 1)
                if q >= 2:
                    pe.wait_ge(v_ready, q - 1)
                for c in range(TC):
                    last = nc.tensor.matmul(v_ps[:, q % 2, c * D:(c + 1) * D], v_sb[:, q, c * P:(c + 1) * P],
                                            wg_sb[:, :], start=(c == 0), stop=(c == TC - 1), skip_group_check=True)
                last.then_inc(v_product, 1)

            def aggregate(b, t, first):
                pe.wait_ge(filtered, b * NT + t + 1)
                if first:
                    pe.wait_ge(v_ready, t + 1)
                for a in range(BANKS):
                    if t == 0 and not first:
                        pe.wait_ge(feat_ready, BANKS * (b - 1) + a + 1)
                    for c in range(TC):
                        last = nc.tensor.matmul(accT[:, a, :], v_sb[:, t, c * D:(c + 1) * D],
                                                ring[:, t % R, c, a * BANK:(a + 1) * BANK],
                                                start=(t == 0 and c == 0), stop=(t == NT - 1 and c == TC - 1))
                    last.then_inc(bank_product, 1)

            def count(b, t):
                pe.wait_ge(marked, b * NT + t + 1)
                for k in range(GROUPS):
                    last = nc.tensor.matmul(counts[:, bass.ds(b * GROUPS + k, 1)], mark[:, t % MARKS, k * P:(k + 1) * P],
                                            ones[:, 0:1], start=(t == 0 and k == 0),
                                            stop=(t == NT - 1 and k == GROUPS - 1), skip_group_check=True)
                last.then_inc(counted, 1)

            def turn_feat(e, groups):
                for k in range(groups):
                    last = nc.tensor.transpose(turned[:, k // TC, (k % TC) * P:(k % TC + 1) * P],
                                               featT[:, k * P:(k + 1) * P], ident[:, :])
                last.then_inc(feat_turned, 1)

            def block_steps(b, first):
                for t in range(NT):
                    aggregate(b, t, first)
                    if t >= COUNT_LAG:
                        count(b, t - COUNT_LAG)
                    elif not first:
                        count(b - 1, t - COUNT_LAG + NT)
                    if not first and t == AT_TURN:
                        pe.wait_ge(feat_ready, BANKS * b)
                        turn_feat(b - 1, GROUPS)
                if not first:
                    pe.wait_ge(added, b)

            pe.wait_ge(weights_loaded, 16 * 5)
            pe.wait_ge(constants_set, 1)
            hidden(0)
            hidden(1)
            for q in range(NT):
                make_v(q)
                if q + 2 < NT:
                    hidden(q + 2)
            block_steps(0, True)
            pe.wait_ge(hidden_ready, NT)
            with pe.Fori(1, NIB) as b:
                block_steps(b, False)
            last_b = NIB - 1
            for t in range(NT - COUNT_LAG, NT):
                count(last_b, t)
            pe.wait_ge(feat_ready, BANKS * NIB)
            turn_feat(last_b, GROUPS)

            pe.wait_ge(flag_step, 2)
            nc.tensor.matmul(counts[:, ROWT:ROWT + 1], ones[:, :], above[:, :], start=True,
                             stop=True).then_inc(rows_above, 1)

            pe.wait_ge(flag_ready, 1)
            with pe.If(pe.value_load(select_flag[0:1, 0:1], min_val=0, max_val=1) > 0):
                with pe.Fori(0, ROWT) as r:
                    pe.wait_ge(cols_filtered, r + 1)
                    pe.wait_ge(added, NIB + r)
                    for q in range(NT):
                        if q >= 2:
                            pe.wait_ge(group_copied, NT * r + q - 1)
                        for c in range(TC):
                            last = nc.tensor.transpose(turned[:, q % 2, c * P:(c + 1) * P],
                                                       cols[:, (q * TC + c) * P:(q * TC + c + 1) * P], ident[:, :])
                        last.then_inc(group_turned, 1)
                    pe.wait_ge(rows_kept, r + 1)
                    for q in range(NT):
                        if q >= 2:
                            pe.wait_ge(group_restored, NT * r + q - 1)
                        for c in range(TC):
                            last = nc.tensor.transpose(turned[:, q % 2, c * P:(c + 1) * P],
                                                       rows[:, (q * TC + c) * P:(q * TC + c + 1) * P], ident[:, :])
                        last.then_inc(group_returned, 1)
                    pe.wait_ge(group_restored, NT * (r + 1))
                    for j in range(NT * TC):
                        last = nc.tensor.matmul(accT[:, 0, 0:P], v_sb[:, j // TC, (j % TC) * D:(j % TC + 1) * D],
                                                cols[:, j * P:(j + 1) * P], start=(j == 0), stop=(j == NT * TC - 1))
                    last.then_inc(select_done, 1)
                    pe.wait_ge(feat_ready, BANKS * NIB + r + 1)
                    turn_feat(NIB + r, 1)


def kernel(x, adj, L0_gnn_W_proj, L0_gnn_b_proj, L0_gnn_W_gcn, L0_gnn_b_gcn):
    import numpy as np
    import concourse.bacc as bacc
    from concourse import mybir as mb
    from concourse.bass_utils import run_bass_kernel_spmd

    n = x.shape[0]
    x = np.asarray(x)
    adj = np.asarray(adj)
    arrays = {
        "adj_tiles": np.ascontiguousarray(
            adj.reshape(n // IB, IB, n // (TC * P), TC, P).transpose(0, 2, 4, 3, 1)),
        "x": np.ascontiguousarray(x),
        "xT": np.ascontiguousarray(x.T),
        "w_proj": np.ascontiguousarray(L0_gnn_W_proj),
        "b_proj": np.ascontiguousarray(np.asarray(L0_gnn_b_proj).reshape(D, 1)),
        "w_gcn": np.ascontiguousarray(L0_gnn_W_gcn),
        "b_gcn": np.ascontiguousarray(np.asarray(L0_gnn_b_gcn).reshape(D, 1)),
        "identity": np.eye(P, dtype=np.float32),
    }
    nc = bacc.Bacc("TRN2", target_bir_lowering=False, num_devices=1)
    aps = {name: nc.dram_tensor(name, a.shape, mb.dt.from_np(a.dtype), kind="ExternalInput").ap()
           for name, a in arrays.items()}
    out = nc.dram_tensor("out", (n, D), mb.dt.float32, kind="ExternalOutput").ap()
    top_k_graph_layer(nc, **aps, out=out)
    result = run_bass_kernel_spmd(nc, [arrays], core_ids=[0])
    return result.results[0]["out"]
```

```python
from contextlib import ExitStack

import concourse.bass as bass
from concourse import mybir

P = 128
D = 128
TOPK = 350
EPS = 1e-5
IB = 1024
TC = 4
BANK = 512
BANKS = IB // BANK
GROUPS = IB // P
SLOTS = 8
FOLD_LAG = 2
ACT_EVEN = (4, 12)

ALU = mybir.AluOpType
ACT = mybir.ActivationFunctionType
F32 = mybir.dt.float32
BF16 = mybir.dt.bfloat16
I32 = mybir.dt.int32
AX_X = mybir.AxisListType.X


def top_k_graph_layer(
    nc: bass.Bass,
    adj_tiles: bass.AP,
    x: bass.AP,
    xT: bass.AP,
    w_proj: bass.AP,
    b_proj: bass.AP,
    w_gcn: bass.AP,
    b_gcn: bass.AP,
    identity: bass.AP,
    out: bass.AP,
):
    N = x.shape[0]
    NIB = N // IB
    NT = N // (TC * P)
    R = min(SLOTS, NT)
    NTILES = NIB * NT
    assert N % IB == 0 and NIB > 2 and NIB % 2 == 0 and NT % R == 0 and NT % 4 == 0 and BANKS == 2 and x.shape[1] == D == P and BANK == TC * P
    ROWT = N // P

    x_rows = x.rearrange("(b k p) d -> b p k d", k=GROUPS, p=P)
    out_rows = out.rearrange("(b k p) d -> b p k d", k=GROUPS, p=P)
    adj_cols = adj_tiles.rearrange("b t p c i -> b p t c i")

    with ExitStack() as ctx:
        def sb(name, shape, dt):
            return ctx.enter_context(nc.sbuf_tensor(name, shape, dt))

        def psum(name, shape, dt):
            return ctx.enter_context(nc.psum_tensor(name, shape, dt))

        def sem(name):
            return ctx.enter_context(nc.semaphore(name))

        ring = sb("ring", [P, R, TC, IB], F32)
        v_sb = sb("v_sb", [P, NT, TC * D], F32)
        pair_sum = sb("pair_sum", [P, 2, 2 * IB], BF16)
        four_sum = sb("four_sum", [P, 2, IB], BF16)
        mark = sb("mark", [P, 2, IB], BF16)
        marks = sb("marks", [P, 2, 2 * IB], BF16)
        ones = sb("ones", [P, P], BF16)
        ident = sb("ident", [P, P], F32)
        wp_sb = sb("wp_sb", [P, D], F32)
        wg_sb = sb("wg_sb", [P, D], F32)
        bias = sb("bias", [P, 2], F32)
        featT = sb("featT", [P, IB], F32)
        x_sb = sb("x_sb", [P, GROUPS, D], F32)
        y_sb = sb("y_sb", [P, GROUPS, D], F32)
        norm_sb = sb("norm_sb", [P, GROUPS, D], F32)
        row_sum = sb("row_sum", [P, GROUPS], F32)
        neg_mean = sb("neg_mean", [P, GROUPS], F32)
        sq_sum = sb("sq_sum", [P, GROUPS], F32)
        var = sb("var", [P, 2, GROUPS], F32)
        moments = sb("moments", [P, GROUPS, 2], F32)
        bn = sb("bn", [P, GROUPS, 6], F32)
        rstd0 = sb("rstd0", [P, GROUPS], F32)
        newton = sb("newton", [P, 4, GROUPS], F32)
        rstd = sb("rstd", [P, GROUPS], F32)
        shift = sb("shift", [P, GROUPS], F32)
        pool_const = sb("pool_const", [P, 5, GROUPS], F32)
        bound = sb("bound", [P, 1], F32)
        above = sb("above", [P, 1], BF16)
        select_flag = sb("select_flag", [P, 1], I32)
        tau = sb("tau", [P, 1], I32)
        candidate = sb("candidate", [P, 1], I32)
        keep_bit = sb("keep_bit", [P, 1], I32)
        bit = sb("bit", [P, 2], F32)
        bit_int = sb("bit_int", [P, 1], I32)
        n_at_least = sb("n_at_least", [P, 1], F32)
        n_above = sb("n_above", [P, 1], F32)
        room = sb("room", [P, 1], F32)

        accT = psum("accT", [P, 2, BANKS, BANK], F32)
        counts = psum("counts", [P, BANK], F32)
        turned = psum("turned", [P, 2, BANK], F32)
        v_ps = accT[:, 1]

        half = NT * TC * P
        flat = ring[:, :, :, :].rearrange("p s c i -> p (s c i)")
        cols = flat[:, 0:half]
        rows = flat[:, half:2 * half]
        prefix = flat[:, 2 * half:3 * half]
        equal = flat[:, 3 * half:3 * half + half // 2].bitcast(BF16)
        passed = flat[:, 3 * half + half // 2:4 * half].bitcast(BF16)

        weights_loaded = sem("weights_loaded")
        xT_loaded = [sem(f"xT_loaded{q}") for q in range(NT)]
        tile_loaded = [sem(f"tile_loaded{s}") for s in range(R)]
        constants_set = sem("constants_set")
        hidden_product = sem("hidden_product")
        hidden_ready = sem("hidden_ready")
        v_product = sem("v_product")
        v_ready = sem("v_ready")
        squared = sem("squared")
        act_squared = sem("act_squared")
        filtered = sem("filtered")
        paired = sem("paired")
        folded = sem("folded")
        marked = sem("marked")
        added_up = sem("added_up")
        counted = sem("counted")
        bank_product = sem("bank_product")
        feat_ready = sem("feat_ready")
        feat_turned = sem("feat_turned")
        x_loaded = sem("x_loaded")
        added = sem("added")
        summed = sem("summed")
        mean_ready = sem("mean_ready")
        sq_summed = sem("sq_summed")
        pool_step = sem("pool_step")
        var_ready = sem("var_ready")
        rstd_ready = sem("rstd_ready")
        shift_ready = sem("shift_ready")
        wp_loaded = sem("wp_loaded")
        half_turned = sem("half_turned")
        half_added = sem("half_added")
        half_measured = sem("half_measured")
        half_aggregated = sem("half_aggregated")
        half_rstd_ready = sem("half_rstd_ready")
        half_normed = sem("half_normed")
        half_stored = [sem(f"half_stored{a}") for a in range(BANKS)]
        normed = sem("normed")
        stored = sem("stored")
        flag_step = sem("flag_step")
        rows_above = sem("rows_above")
        flag_ready = sem("flag_ready")
        cols_loaded = sem("cols_loaded")
        cols_squared = sem("cols_squared")
        cols_filtered = sem("cols_filtered")
        group_turned = sem("group_turned")
        group_copied = sem("group_copied")
        search_step = sem("search_step")
        rows_kept = sem("rows_kept")
        group_returned = sem("group_returned")
        group_restored = sem("group_restored")
        select_done = sem("select_done")

        ACT_TILES = [t for t in range(NT) if t % 2 == 1 or t in ACT_EVEN]

        EARLY_TANH = {NT // 2: 0, NT - 3: 1}
        EARLY = len(EARLY_TANH)

        POOL_STEPS = 6
        POOL_CONSTS = (-1.0 / D, 1.0 / D, EPS, -0.5, 1.5)

        EPILOGUES = NIB - 1
        PAIRS = (NIB - 2) // 2

        AT_EVACUATE, AT_TURN, AT_COUNT, AT_ADD, AT_SUM, AT_SQUARE, AT_NORM = (
            (3, 3, 5, 6, 7, 9, 11) if NT >= 16 else (1, 2, 2, 3, 3, 4, 5))

        def fixed(b, value):
            return isinstance(b, int) and b == value

        def run_blocks(engine, block_steps):
            block_steps(0, 0)
            with engine.Fori(0, PAIRS) as n:
                block_steps(2 * n + 1, 1)
                block_steps(2 * n + 2, 0)
            block_steps(NIB - 1, 1)

        def load_x(sp, source, groups):
            sp.dma_start(x_sb[:, 0:groups, :], source).then_inc(x_loaded, 16)

        def add_x(dve, e, groups, loads):
            dve.wait_ge(feat_turned, e + 1)
            dve.wait_ge(x_loaded, 16 * loads)
            nc.vector.tensor_tensor(
                y_sb[:, 0:groups, :], turned[:, :, :].rearrange("p a (k d) -> p (a k) d", d=D)[:, 0:groups, :],
                x_sb[:, 0:groups, :], ALU.add).then_inc(added, 1)

        def sum_rows(act, e, groups):
            act.wait_ge(added, e + 1)
            for k in range(groups):
                last = nc.scalar.activation(norm_sb[:, k, :], y_sb[:, k, :], ACT.Identity,
                                            accum_out=row_sum[:, k:k + 1])
            last.then_inc(summed, 1)

        def sum_squares(act, e, groups):
            act.wait_ge(mean_ready, e + 1)
            for k in range(groups):
                last = nc.scalar.activation(norm_sb[:, k, :], y_sb[:, k, :], ACT.Square,
                                            bias=neg_mean[:, k:k + 1], accum_out=sq_sum[:, k:k + 1])
            last.then_inc(sq_summed, 1)

        def normalise(act, e, target, groups):
            act.wait_ge(shift_ready, e + 1)
            for k in range(groups):
                last = nc.scalar.activation(norm_sb[:, k, :], y_sb[:, k, :], ACT.Identity,
                                            bias=shift[:, k:k + 1], scale=rstd[:, k:k + 1])
            last.then_inc(normed, 1)
            act.wait_ge(normed, e + 1)
            act.dma_start(target, norm_sb[:, 0:groups, :]).then_inc(stored, 16)

        def half(a):
            return slice(a * TC, (a + 1) * TC)

        def inverse_deviation(pool, variance, n, g, done):
            eps, minus_half, three_halves = (pool_const[:, c, g] for c in (2, 3, 4))
            nc.gpsimd.tensor_tensor(var[:, 1, g], variance, eps, ALU.add).then_inc(pool_step, 1)
            pool.wait_ge(pool_step, POOL_STEPS * n + 1)
            nc.gpsimd.tensor_tensor(rstd0[:, g], var[:, 1, g], minus_half, ALU.pow).then_inc(pool_step, 1)
            nc.gpsimd.tensor_tensor(newton[:, 0, g], var[:, 1, g], minus_half, ALU.mult).then_inc(pool_step, 1)
            pool.wait_ge(pool_step, POOL_STEPS * n + 3)
            nc.gpsimd.tensor_tensor(newton[:, 1, g], newton[:, 0, g], rstd0[:, g], ALU.mult).then_inc(pool_step, 1)
            pool.wait_ge(pool_step, POOL_STEPS * n + 4)
            nc.gpsimd.tensor_tensor(newton[:, 2, g], newton[:, 1, g], rstd0[:, g], ALU.mult).then_inc(pool_step, 1)
            pool.wait_ge(pool_step, POOL_STEPS * n + 5)
            nc.gpsimd.tensor_tensor(newton[:, 3, g], newton[:, 2, g], three_halves, ALU.add).then_inc(pool_step, 1)
            pool.wait_ge(pool_step, POOL_STEPS * n + 6)
            nc.gpsimd.tensor_tensor(rstd[:, g], newton[:, 3, g], rstd0[:, g], ALU.mult).then_inc(done, 1)

        def statistics(pool, e, n, groups):
            g = slice(0, groups)
            minus_1_d, one_d = (pool_const[:, c, g] for c in (0, 1))
            pool.wait_ge(summed, e + 1)
            nc.gpsimd.tensor_tensor(neg_mean[:, g], row_sum[:, g], minus_1_d, ALU.mult).then_inc(mean_ready, 1)
            pool.wait_ge(sq_summed, e + 1)
            nc.gpsimd.tensor_tensor(var[:, 0, g], sq_sum[:, g], one_d, ALU.mult).then_inc(var_ready, 1)
            pool.wait_ge(var_ready, e + 1)
            inverse_deviation(pool, var[:, 0, g], n, g, rstd_ready)
            pool.wait_ge(rstd_ready, e + 1)
            nc.gpsimd.tensor_tensor(shift[:, g], neg_mean[:, g], rstd[:, g], ALU.mult).then_inc(shift_ready, 1)

        block = ctx.enter_context(nc.Block())

        @block.sync
        def _(sp):
            def load_tile(b, t, freed):
                s = t % R
                T = b * NT + t
                if freed:
                    sp.wait_ge(bank_product, BANKS * (T - R + 1))
                    sp.wait_ge(paired, T - R + 1)
                sp.dma_start(ring[:, s, :, :], adj_tiles[b, t]).then_inc(tile_loaded[s], 16)

            sp.dma_start(wp_sb[:, :], w_proj).then_inc(wp_loaded, 16)
            for q in range(NT):
                sp.dma_start(v_sb[:, q, :], xT[:, q * TC * P:(q + 1) * TC * P]).then_inc(xT_loaded[q], 16)
                if q == NT // 4:
                    load_tile(0, 0, False)
            for t in range(1, NT):
                load_tile(0, t, t >= R)
            with sp.Fori(1, NIB) as b:
                load_x(sp, x_rows[b - 1], GROUPS)
                for t in range(NT):
                    if t == NT - 1:
                        sp.wait_ge(added, b)
                    load_tile(b, t, True)
            sp.wait_ge(added, NIB - 1)
            load_x(sp, x_rows[NIB - 1], GROUPS)

            sp.wait_ge(flag_ready, 1)
            with sp.If(sp.value_load(select_flag[0:1, 0:1], min_val=0, max_val=1) > 0):
                with sp.Fori(0, NIB) as b:
                    with sp.Fori(0, GROUPS) as k:
                        r = b * GROUPS + k
                        sp.wait_ge(added, EPILOGUES + r)
                        for t in range(NT):
                            sp.dma_start(cols.rearrange("p (t c i) -> p t c i", t=NT, c=TC)[:, t],
                                         adj_tiles[b, t, :, :, bass.ds(k * P, P)]).then_inc(cols_loaded, 16)
                        load_x(sp, x_rows[b, :, bass.ds(k, 1), :], 1)

        @block.gpsimd
        def _(pool):
            nc.gpsimd.memset(ones[:, :], 1.0).then_inc(constants_set, 1)
            for n, value in enumerate(POOL_CONSTS):
                nc.gpsimd.memset(pool_const[:, n, :], value).then_inc(constants_set, 1)
            pool.wait_ge(constants_set, 1 + len(POOL_CONSTS))
            with pool.Fori(0, EPILOGUES) as b:
                statistics(pool, b, b, GROUPS)
            for a in range(BANKS):
                pool.wait_ge(half_aggregated, a + 1)
                inverse_deviation(pool, moments[:, half(a), 1], EPILOGUES + a, half(a), half_rstd_ready)

            pool.wait_ge(flag_ready, 1)
            with pool.If(pool.value_load(select_flag[0:1, 0:1], min_val=0, max_val=1) > 0):
                with pool.Fori(0, ROWT) as r:
                    statistics(pool, EPILOGUES + r, EPILOGUES + BANKS + r, 1)

        @block.scalar
        def _(act):
            def hidden(q):
                act.wait_ge(hidden_product, q + 1)
                nc.scalar.activation(v_sb[:, q, :], turned[:, q % 2, :], ACT.Tanh,
                                     bias=bias[:, 0:1]).then_inc(hidden_ready, 1)

            def tanh_tile(b, t):
                act.wait_ge(squared, b * NT + t + 1)
                if t in ACT_TILES:
                    nc.scalar.activation(ring[:, t % R, :, :], ring[:, t % R, :, :],
                                         ACT.Square).then_inc(act_squared, 1)
                    act.wait_ge(act_squared, len(ACT_TILES) * b + ACT_TILES.index(t) + 1)
                nc.scalar.activation(ring[:, t % R, :, :], ring[:, t % R, :, :], ACT.Tanh).then_inc(filtered, 1)

            def copy_v(q):
                act.wait_ge(v_product, q + 1)
                nc.scalar.copy(v_sb[:, q, :], v_ps[:, q % 2, :]).then_inc(v_ready, 1)

            def evacuate(b, parity):
                for a in range(BANKS):
                    act.wait_ge(bank_product, BANKS * ((b + 1) * NT - 1) + a + 1)
                    nc.scalar.activation(featT[:, a * BANK:(a + 1) * BANK], accT[:, parity, a, :], ACT.Relu,
                                         bias=bias[:, 1:2]).then_inc(feat_ready, 1)

            def block_steps(b, parity):
                first = fixed(b, 0)
                for t in range(NT):
                    if not first or t >= EARLY:
                        tanh_tile(b, t)
                    if not first:
                        if t == AT_EVACUATE:
                            evacuate(b - 1, 1 - parity)
                        if t == AT_SUM:
                            sum_rows(act, b - 1, GROUPS)
                        if t == AT_SQUARE:
                            sum_squares(act, b - 1, GROUPS)
                        if t == AT_NORM:
                            normalise(act, b - 1, out_rows[b - 1], GROUPS)
                if not first:
                    act.wait_ge(feat_turned, b)
                    act.wait_ge(stored, 16 * b)

            for dst, src in ((wg_sb[:, :], w_gcn), (bias[:, 0:1], b_proj), (bias[:, 1:2], b_gcn),
                             (ident[:, :], identity)):
                act.dma_start(dst, src).then_inc(weights_loaded, 16)
            act.wait_ge(weights_loaded, 16 * 4)
            hidden(0)
            hidden(1)
            for q in range(NT):
                copy_v(q)
                if q + 2 < NT:
                    hidden(q + 2)
                if q in EARLY_TANH:
                    tanh_tile(0, EARLY_TANH[q])
            run_blocks(act, block_steps)
            last_b = NIB - 1
            evacuate(last_b, 1)
            for a in range(BANKS):
                act.wait_ge(half_normed, a + 1)
                act.dma_start(out_rows[last_b, :, half(a), :], norm_sb[:, half(a), :]).then_inc(half_stored[a], 16)
            for a in range(BANKS):
                act.wait_ge(half_stored[a], 16)

            act.wait_ge(flag_ready, 1)
            with act.If(act.value_load(select_flag[0:1, 0:1], min_val=0, max_val=1) > 0):
                with act.Fori(0, NIB) as b:
                    with act.Fori(0, GROUPS) as k:
                        r = b * GROUPS + k
                        e = EPILOGUES + r
                        act.wait_ge(cols_squared, r + 1)
                        nc.scalar.activation(cols, cols, ACT.Tanh).then_inc(cols_filtered, 1)
                        act.wait_ge(select_done, r + 1)
                        nc.scalar.activation(featT[:, 0:P], accT[:, 0, 0, 0:P], ACT.Relu,
                                             bias=bias[:, 1:2]).then_inc(feat_ready, 1)
                        sum_rows(act, e, 1)
                        sum_squares(act, e, 1)
                        normalise(act, e, out_rows[b, :, bass.ds(k, 1), :], 1)
                        act.wait_ge(stored, 16 * (e + 1))

        @block.vector
        def _(dve):
            def square_tile(b, t):
                s = t % R
                dve.wait_ge(tile_loaded[s], 16 * (b * (NT // R) + t // R + 1))
                if t in ACT_TILES:
                    nc.vector.tensor_scalar(ring[:, s, :, :], ring[:, s, :, :], 0.0, None, ALU.max).then_inc(squared, 1)
                    return
                nc.vector.scalar_tensor_tensor(out=ring[:, s, :, :], in0=ring[:, s, :, :], scalar=0.0,
                                               in1=ring[:, s, :, :], op0=ALU.max, op1=ALU.mult).then_inc(squared, 1)

            def fold_tiles(b, t, parity, later):
                n = b * (NT // 2) + t // 2
                s = t % R
                block_marks = marks[:, parity, :]
                tiles = ring[:, s - 1:s + 1, :, :].rearrange("p s (h c) i -> p s h (c i)", h=2)
                dve.wait_ge(filtered, b * NT + t + 1)
                if later or t > 1:
                    dve.wait_ge(folded, n)
                nc.vector.tensor_tensor(pair_sum[:, :, :], tiles[:, :, 0, :], tiles[:, :, 1, :],
                                        ALU.add).then_inc(paired, 2)
                dve.wait_ge(paired, 2 * (n + 1))
                if later or t > 1:
                    dve.wait_ge(marked, n)
                nc.vector.tensor_tensor(four_sum[:, :, :], pair_sum[:, :, 0:IB], pair_sum[:, :, IB:2 * IB],
                                        ALU.add).then_inc(folded, 1)
                dve.wait_ge(folded, n + 1)
                if t == 1:
                    nc.vector.tensor_scalar(block_marks, four_sum[:, :, :].rearrange("p s i -> p (s i)"), 0.0, None,
                                            ALU.is_gt).then_inc(marked, 1)
                    return
                if later or t > 3:
                    dve.wait_ge(added_up, b * (NT // 2 - 1) + t // 2 - 1)
                nc.vector.tensor_scalar(mark[:, :, :], four_sum[:, :, :], 0.0, None, ALU.is_gt).then_inc(marked, 1)
                dve.wait_ge(marked, n + 1)
                nc.vector.tensor_tensor(block_marks, block_marks, mark[:, :, :].rearrange("p s i -> p (s i)"),
                                        ALU.add).then_inc(added_up, 1)

            def block_steps(b, parity):
                first = fixed(b, 0)
                for t in range(NT):
                    square_tile(b, t)
                    folding = t - FOLD_LAG
                    if folding > 0 and folding % 2:
                        fold_tiles(b, folding, parity, not first)
                    elif folding == -1 and not first:
                        fold_tiles(b - 1, NT - 1, 1 - parity, True)
                    if not first and t == AT_ADD:
                        add_x(dve, b - 1, GROUPS, b)
                if not first:
                    dve.wait_ge(normed, b)
                    dve.wait_ge(counted, b)

            last_b = NIB - 1
            run_blocks(dve, block_steps)
            fold_tiles(last_b, NT - 1, 1, True)
            dve.wait_ge(x_loaded, 16 * NIB)
            for a in range(BANKS):
                dve.wait_ge(half_turned, a + 1)
                nc.vector.tensor_tensor(y_sb[:, half(a), :], turned[:, a, :].rearrange("p (k d) -> p k d", d=D),
                                        x_sb[:, half(a), :], ALU.add).then_inc(half_added, 1)
                dve.wait_ge(half_added, a + 1)
                for k in range(a * TC, (a + 1) * TC):
                    last = nc.vector.bn_stats(bn[:, k, :], y_sb[:, k, :])
                last.then_inc(half_measured, 1)
                dve.wait_ge(half_measured, a + 1)
                for k in range(a * TC, (a + 1) * TC):
                    last = nc.vector.bn_aggr(moments[:, k, :], bn[:, k, :])
                last.then_inc(half_aggregated, 1)
            dve.wait_ge(stored, 16 * EPILOGUES)
            for a in range(BANKS):
                dve.wait_ge(half_rstd_ready, a + 1)
                for k in range(a * TC, (a + 1) * TC):
                    last = nc.vector.tensor_scalar(norm_sb[:, k, :], y_sb[:, k, :], moments[:, k, 0:1],
                                                   rstd[:, k:k + 1], ALU.subtract, ALU.mult)
                last.then_inc(half_normed, 1)
            dve.wait_ge(counted, NIB)
            nc.vector.reduce_max(bound[:, 0:1], counts[:, 0:ROWT], AX_X).then_inc(flag_step, 1)
            dve.wait_ge(flag_step, 1)
            nc.vector.tensor_scalar(above[:, :], bound[:, 0:1], TOPK / TC, None, ALU.is_gt).then_inc(flag_step, 1)
            dve.wait_ge(rows_above, 1)
            nc.vector.tensor_scalar(select_flag[:, :], counts[:, ROWT:ROWT + 1], 0.5, None,
                                    ALU.is_gt).then_inc(flag_ready, 1)

            dve.wait_ge(flag_ready, 1)
            with dve.If(dve.value_load(select_flag[0:1, 0:1], min_val=0, max_val=1) > 0):
                BITS = 30
                STEPS = 6 * BITS + 8
                with dve.Fori(0, ROWT) as r:
                    dve.wait_ge(cols_loaded, 16 * NT * (r + 1))
                    nc.vector.scalar_tensor_tensor(out=cols, in0=cols, scalar=0.0, in1=cols, op0=ALU.max,
                                                   op1=ALU.mult).then_inc(cols_squared, 1)
                    for q in range(NT):
                        dve.wait_ge(group_turned, NT * r + q + 1)
                        nc.vector.tensor_copy(rows[:, q * BANK:(q + 1) * BANK], turned[:, q % 2, :]).then_inc(group_copied, 1)
                    nc.vector.memset(tau[:, :], 0).then_inc(search_step, 1)
                    dve.wait_ge(group_copied, NT * (r + 1))
                    nc.vector.memset(bit[:, 0:1], float(2 ** (BITS - 1))).then_inc(search_step, 1)
                    with dve.Fori(0, BITS) as n:
                        s0 = STEPS * r + 6 * n + 2
                        dve.wait_ge(search_step, s0)
                        nc.vector.tensor_copy(bit_int[:, :], bit[:, 0:1]).then_inc(search_step, 1)
                        dve.wait_ge(search_step, s0 + 1)
                        nc.vector.tensor_tensor(candidate[:, :], tau[:, :], bit_int[:, :],
                                                ALU.bitwise_or).then_inc(search_step, 1)
                        dve.wait_ge(search_step, s0 + 2)
                        nc.vector.tensor_scalar(passed, rows, candidate[:, :].bitcast(F32), None, ALU.is_ge, ALU.add,
                                                accum_out=n_at_least[:, :]).then_inc(search_step, 1)
                        dve.wait_ge(search_step, s0 + 3)
                        nc.vector.scalar_tensor_tensor(out=keep_bit[:, :], in0=n_at_least[:, :], scalar=float(TOPK),
                                                       in1=bit[:, 0:1], op0=ALU.is_ge, op1=ALU.mult).then_inc(search_step, 1)
                        dve.wait_ge(search_step, s0 + 4)
                        nc.vector.tensor_tensor(tau[:, :], tau[:, :], keep_bit[:, :], ALU.bitwise_or).then_inc(search_step, 1)
                        nc.vector.tensor_scalar(bit[:, 0:1], bit[:, 0:1], 0.5, None, ALU.mult).then_inc(search_step, 1)
                    s1 = STEPS * r + 6 * BITS + 2
                    tau_f = tau[:, :].bitcast(F32)
                    dve.wait_ge(search_step, s1)
                    nc.vector.tensor_scalar(passed, rows, tau_f, None, ALU.is_gt, ALU.add,
                                            accum_out=n_above[:, :]).then_inc(search_step, 1)
                    nc.vector.tensor_scalar(equal, rows, tau_f, None, ALU.is_equal).then_inc(search_step, 1)
                    dve.wait_ge(search_step, s1 + 2)
                    nc.vector.tensor_scalar(room[:, :], n_above[:, :], -1.0, float(TOPK), ALU.mult,
                                            ALU.add).then_inc(search_step, 1)
                    nc.vector.tensor_tensor_scan(prefix, equal, equal, 0.0, ALU.add, ALU.bypass).then_inc(search_step, 1)
                    dve.wait_ge(search_step, s1 + 4)
                    nc.vector.scalar_tensor_tensor(out=passed, in0=prefix, scalar=room[:, 0:1], in1=equal,
                                                   op0=ALU.is_le, op1=ALU.mult).then_inc(search_step, 1)
                    dve.wait_ge(search_step, s1 + 5)
                    nc.vector.scalar_tensor_tensor(out=prefix, in0=rows, scalar=tau_f, in1=passed,
                                                   op0=ALU.is_gt, op1=ALU.add).then_inc(search_step, 1)
                    dve.wait_ge(search_step, s1 + 6)
                    nc.vector.tensor_tensor(rows, rows, prefix, ALU.mult).then_inc(rows_kept, 1)
                    for q in range(NT):
                        dve.wait_ge(group_returned, NT * r + q + 1)
                        nc.vector.tensor_copy(cols[:, q * BANK:(q + 1) * BANK], turned[:, q % 2, :]).then_inc(group_restored, 1)
                    add_x(dve, EPILOGUES + r, 1, NIB + r + 1)
                    dve.wait_ge(normed, EPILOGUES + r + 1)

        @block.tensor
        def _(pe):
            def hidden(q):
                pe.wait_ge(xT_loaded[q], 16)
                if q >= 2:
                    pe.wait_ge(hidden_ready, q - 1)
                nc.tensor.matmul(turned[:, q % 2, :], wp_sb[:, :], v_sb[:, q, :], start=True,
                                 stop=True).then_inc(hidden_product, 1)

            def make_v(q):
                pe.wait_ge(hidden_ready, q + 1)
                if q >= 2:
                    pe.wait_ge(v_ready, q - 1)
                for c in range(TC):
                    last = nc.tensor.matmul(v_ps[:, q % 2, c * D:(c + 1) * D], v_sb[:, q, c * P:(c + 1) * P],
                                            wg_sb[:, :], start=(c == 0), stop=(c == TC - 1), skip_group_check=True)
                last.then_inc(v_product, 1)

            def aggregate(b, t, parity, first, turn_early):
                pe.wait_ge(filtered, b * NT + t + 1)
                if first:
                    pe.wait_ge(v_ready, t + 1)
                by_bank = [(a, c) for a in range(BANKS) for c in range(TC)]
                by_chunk = [(a, c) for c in range(TC) for a in range(BANKS)]
                for a, c in by_bank if t in (0, NT - 1) else by_chunk:
                    last = nc.tensor.matmul(accT[:, parity, a, :], v_sb[:, t, c * D:(c + 1) * D],
                                            ring[:, t % R, c, a * BANK:(a + 1) * BANK],
                                            start=(t == 0 and c == 0), stop=(t == NT - 1 and c == TC - 1))
                    if c == TC - 1:
                        last.then_inc(bank_product, 1)
                    if turn_early and (a, c) == (BANKS - 1, TC // 2 - 1):
                        turn_half(0, b)

            def count(b, parity):
                pe.wait_ge(added_up, (NT // 2 - 1) * (b + 1))
                for k in range(GROUPS):
                    for n in range(2):
                        last = nc.tensor.matmul(counts[:, bass.ds(b * GROUPS + k, 1)],
                                                marks[:, parity, n * IB + k * P:n * IB + (k + 1) * P],
                                                ones[:, 0:1], start=(n == 0), stop=(n == 1))
                last.then_inc(counted, 1)

            def turn_feat(e, groups):
                for k in range(groups):
                    last = nc.tensor.transpose(turned[:, k // TC, (k % TC) * P:(k % TC + 1) * P],
                                               featT[:, k * P:(k + 1) * P], ident[:, :])
                last.then_inc(feat_turned, 1)

            def turn_half(a, b):
                pe.wait_ge(feat_ready, BANKS * b + a + 1)
                for k in range(TC):
                    last = nc.tensor.transpose(turned[:, a, k * P:(k + 1) * P],
                                               featT[:, (a * TC + k) * P:(a * TC + k + 1) * P], ident[:, :])
                last.then_inc(half_turned, 1)

            def block_steps(b, parity):
                first = fixed(b, 0)
                for t in range(NT):
                    aggregate(b, t, parity, first, fixed(b, NIB - 1) and t == NT - 1)
                    if not first and t == AT_TURN:
                        pe.wait_ge(feat_ready, BANKS * b)
                        turn_feat(b - 1, GROUPS)
                    if not first and t == AT_COUNT:
                        count(b - 1, 1 - parity)
                    if not first and t == NT - 2:
                        pe.wait_ge(added, b)

            pe.wait_ge(wp_loaded, 16)
            hidden(0)
            hidden(1)
            pe.wait_ge(weights_loaded, 16 * 4)
            pe.wait_ge(constants_set, 1)
            for q in range(NT):
                make_v(q)
                if q + 2 < NT:
                    hidden(q + 2)
            last_b = NIB - 1
            run_blocks(pe, block_steps)
            turn_half(1, last_b)
            count(last_b, 1)

            pe.wait_ge(flag_step, 2)
            nc.tensor.matmul(counts[:, ROWT:ROWT + 1], ones[:, :], above[:, :], start=True,
                             stop=True).then_inc(rows_above, 1)

            pe.wait_ge(flag_ready, 1)
            with pe.If(pe.value_load(select_flag[0:1, 0:1], min_val=0, max_val=1) > 0):
                with pe.Fori(0, ROWT) as r:
                    pe.wait_ge(cols_filtered, r + 1)
                    pe.wait_ge(added, EPILOGUES + r)
                    for q in range(NT):
                        if q >= 2:
                            pe.wait_ge(group_copied, NT * r + q - 1)
                        for c in range(TC):
                            last = nc.tensor.transpose(turned[:, q % 2, c * P:(c + 1) * P],
                                                       cols[:, (q * TC + c) * P:(q * TC + c + 1) * P], ident[:, :])
                        last.then_inc(group_turned, 1)
                    pe.wait_ge(rows_kept, r + 1)
                    for q in range(NT):
                        if q >= 2:
                            pe.wait_ge(group_restored, NT * r + q - 1)
                        for c in range(TC):
                            last = nc.tensor.transpose(turned[:, q % 2, c * P:(c + 1) * P],
                                                       rows[:, (q * TC + c) * P:(q * TC + c + 1) * P], ident[:, :])
                        last.then_inc(group_returned, 1)
                    pe.wait_ge(group_restored, NT * (r + 1))
                    for j in range(NT * TC):
                        last = nc.tensor.matmul(accT[:, 0, 0, 0:P], v_sb[:, j // TC, (j % TC) * D:(j % TC + 1) * D],
                                                cols[:, j * P:(j + 1) * P], start=(j == 0), stop=(j == NT * TC - 1))
                    last.then_inc(select_done, 1)
                    pe.wait_ge(feat_ready, BANKS * NIB + r + 1)
                    turn_feat(EPILOGUES + r, 1)


def kernel(x, adj, L0_gnn_W_proj, L0_gnn_b_proj, L0_gnn_W_gcn, L0_gnn_b_gcn):
    import numpy as np
    import concourse.bacc as bacc
    from concourse import mybir as mb
    from concourse.bass_utils import run_bass_kernel_spmd

    n = x.shape[0]
    x = np.asarray(x)
    adj = np.asarray(adj)
    arrays = {
        "adj_tiles": np.ascontiguousarray(
            adj.reshape(n // IB, IB, n // (TC * P), TC, P).transpose(0, 2, 4, 3, 1)),
        "x": np.ascontiguousarray(x),
        "xT": np.ascontiguousarray(x.T),
        "w_proj": np.ascontiguousarray(L0_gnn_W_proj),
        "b_proj": np.ascontiguousarray(np.asarray(L0_gnn_b_proj).reshape(D, 1)),
        "w_gcn": np.ascontiguousarray(L0_gnn_W_gcn),
        "b_gcn": np.ascontiguousarray(np.asarray(L0_gnn_b_gcn).reshape(D, 1)),
        "identity": np.eye(P, dtype=np.float32),
    }
    nc = bacc.Bacc("TRN2", target_bir_lowering=False, num_devices=1)
    aps = {name: nc.dram_tensor(name, a.shape, mb.dt.from_np(a.dtype), kind="ExternalInput").ap()
           for name, a in arrays.items()}
    out = nc.dram_tensor("out", (n, D), mb.dt.float32, kind="ExternalOutput").ap()
    top_k_graph_layer(nc, **aps, out=out)
    result = run_bass_kernel_spmd(nc, [arrays], core_ids=[0])
    return result.results[0]["out"]
```
